# Optimizing a Trainium2 kernel written in Bass

```python
import numpy as np
import jax
import jax.numpy as jnp

def _softmax(x, axis=-1):
    return jax.nn.softmax(x, axis=axis)

def _gelu(x):
    return jax.nn.gelu(x, approximate=True)

def _silu(x):
    return jax.nn.silu(x)

def _sigmoid(x):
    return jax.nn.sigmoid(x)

def _layernorm(x, axis=-1, eps=1e-05):
    m = jnp.mean(x, axis=axis, keepdims=True)
    v = jnp.var(x, axis=axis, keepdims=True)
    return (x - m) / jnp.sqrt(v + eps)

def _scatter_add(tgt, idx, src, axis=0):
    return tgt.at[idx].add(src)

def _segment_sum(src, seg, n):
    return jax.ops.segment_sum(src, seg, n)
kernel_name = 'mk_gnn_resnorm_d1_gnn_r32_a475a3'

def setup_inputs(seed: int=0):
    np.random.seed(seed)
    _w = jnp.asarray

    def _rec_inputs():
        import jax
        import jax.numpy as jnp
        _gk = jax.random.key(seed)
        x = -0.000202 + 1 * jax.random.normal(jax.random.fold_in(_gk, 1), (3125, 128), jnp.float32)
        _s = jax.random.randint(jax.random.fold_in(_gk, 2), (25000,), 0, 3125, jnp.int32)
        _d = jax.random.randint(jax.random.fold_in(_gk, 3), (25000,), 0, 3125, jnp.int32)
        _loop = jnp.arange(3125, dtype=jnp.int32)
        src = jnp.concatenate([_s, _d, _loop])
        dst = jnp.concatenate([_d, _s, _loop])
        _o = jnp.argsort(dst, stable=True)
        src = src[_o]
        dst = dst[_o]
        edge_attr_64 = 0.000189758 + 1.00013 * jax.random.normal(jax.random.fold_in(_gk, 11), (53125, 64), jnp.float32)
        return (x, src, dst, edge_attr_64)
    x, src, dst, edge_attr_64 = _rec_inputs()

    def _L0_gnn_setup():
        import jax, jax.numpy as jnp
        import numpy as np
        N_NODES = 50000
        N_EDGES = 25000
        IN_CH = 128
        HID = 128
        EDGE_DIM = 64
        N_LAYERS = 3
        BN_EPS = 1e-05
        LN_EPS = 1e-05

        def _layer_norm(x, g, b):
            mu = jnp.mean(x, axis=-1, keepdims=True)
            var = jnp.mean(jnp.square(x - mu), axis=-1, keepdims=True)
            return (x - mu) * jax.lax.rsqrt(var + LN_EPS) * g + b
        key = jax.random.key(seed)
        ks = jax.random.split(key, 16)
        s = 1.0 / np.sqrt(HID)
        inp = {'feature_vector': jax.random.normal(ks[0], (N_NODES, IN_CH), jnp.float32), 'adj_index': jax.random.randint(ks[1], (2, N_EDGES), 0, N_NODES, jnp.int64) if jax.config.jax_enable_x64 else jax.random.randint(ks[1], (2, N_EDGES), 0, N_NODES, jnp.int32), 'edge_vector': jax.random.normal(ks[2], (N_EDGES, EDGE_DIM), jnp.float32), 'eps': jnp.zeros((N_LAYERS,), jnp.float32), 'edge_W': jax.random.normal(ks[3], (N_LAYERS, EDGE_DIM, IN_CH), jnp.float32) * (1.0 / np.sqrt(EDGE_DIM)), 'edge_b': jnp.zeros((N_LAYERS, IN_CH), jnp.float32), 'W1': jax.random.normal(ks[4], (N_LAYERS, IN_CH, HID), jnp.float32) * s, 'b1': jnp.zeros((N_LAYERS, HID), jnp.float32), 'bn_g': jnp.ones((N_LAYERS, HID), jnp.float32), 'bn_b': jnp.zeros((N_LAYERS, HID), jnp.float32), 'bn_mean': jnp.zeros((N_LAYERS, HID), jnp.float32), 'bn_var': jnp.ones((N_LAYERS, HID), jnp.float32), 'W2': jax.random.normal(ks[5], (N_LAYERS, HID, HID), jnp.float32) * s, 'b2': jnp.zeros((N_LAYERS, HID), jnp.float32), 'ln_g': jnp.ones((HID,), jnp.float32), 'ln_b': jnp.zeros((HID,), jnp.float32)}
        return inp
    _L0_gnn_all = _L0_gnn_setup()
    _L0_gnn_in = {k: v for k, v in _L0_gnn_all.items() if k in ('eps', 'edge_W', 'edge_b', 'W1', 'b1', 'bn_g', 'bn_b', 'bn_mean', 'bn_var', 'W2', 'b2', 'ln_g', 'ln_b')}
    del _L0_gnn_all
    return {'x': x, 'src': src, 'dst': dst, 'edge_attr_64': edge_attr_64, 'L0_gnn_eps': _L0_gnn_in['eps'], 'L0_gnn_edge_W': _L0_gnn_in['edge_W'], 'L0_gnn_edge_b': _L0_gnn_in['edge_b'], 'L0_gnn_W1': _L0_gnn_in['W1'], 'L0_gnn_b1': _L0_gnn_in['b1'], 'L0_gnn_bn_g': _L0_gnn_in['bn_g'], 'L0_gnn_bn_b': _L0_gnn_in['bn_b'], 'L0_gnn_bn_mean': _L0_gnn_in['bn_mean'], 'L0_gnn_bn_var': _L0_gnn_in['bn_var'], 'L0_gnn_W2': _L0_gnn_in['W2'], 'L0_gnn_b2': _L0_gnn_in['b2'], 'L0_gnn_ln_g': _L0_gnn_in['ln_g'], 'L0_gnn_ln_b': _L0_gnn_in['ln_b']}

def reference(x, src, dst, edge_attr_64, L0_gnn_eps, L0_gnn_edge_W, L0_gnn_edge_b, L0_gnn_W1, L0_gnn_b1, L0_gnn_bn_g, L0_gnn_bn_b, L0_gnn_bn_mean, L0_gnn_bn_var, L0_gnn_W2, L0_gnn_b2, L0_gnn_ln_g, L0_gnn_ln_b):
    import jax
    import jax.numpy as jnp

    def _L0_gnn_ref(feature_vector, adj_index, edge_vector, eps, edge_W, edge_b, W1, b1, bn_g, bn_b, bn_mean, bn_var, W2, b2, ln_g, ln_b):
        import jax, jax.numpy as jnp
        import numpy as np
        N_NODES = 50000
        N_EDGES = 25000
        IN_CH = 128
        HID = 128
        EDGE_DIM = 64
        N_LAYERS = 3
        BN_EPS = 1e-05
        LN_EPS = 1e-05

        def _layer_norm(x, g, b):
            mu = jnp.mean(x, axis=-1, keepdims=True)
            var = jnp.mean(jnp.square(x - mu), axis=-1, keepdims=True)
            return (x - mu) * jax.lax.rsqrt(var + LN_EPS) * g + b
        src, dst = (adj_index[0], adj_index[1])
        n = feature_vector.shape[0]
        x = feature_vector
        for k in range(N_LAYERS):
            e = edge_vector @ edge_W[k] + edge_b[k]
            msg = jax.nn.relu(x[src] + e)
            agg = jax.ops.segment_sum(msg, dst, num_segments=n)
            z = (1.0 + eps[k]) * x + agg
            h = z @ W1[k] + b1[k]
            h = (h - bn_mean[k]) * jax.lax.rsqrt(bn_var[k] + BN_EPS) * bn_g[k] + bn_b[k]
            h = jax.nn.relu(h)
            x = h @ W2[k] + b2[k]
            x = jax.nn.relu(_layer_norm(x, ln_g, ln_b))
        return x
    edge_index = jnp.stack([src, dst])
    x = _layernorm(x + _L0_gnn_ref(x, edge_index, edge_attr_64, L0_gnn_eps, L0_gnn_edge_W, L0_gnn_edge_b, L0_gnn_W1, L0_gnn_b1, L0_gnn_bn_g, L0_gnn_bn_b, L0_gnn_bn_mean, L0_gnn_bn_var, L0_gnn_W2, L0_gnn_b2, L0_gnn_ln_g, L0_gnn_ln_b), axis=-1)
    return x

_drawn_inputs = setup_inputs


def setup_inputs(seed=0):
    import zlib

    import numpy as np

    out = dict(_drawn_inputs(seed))
    spreads = {'L0_gnn_eps': (0.0, 2.0),
     'L0_gnn_edge_b': (0.0, 0.1),
     'L0_gnn_b1': (0.0, 0.8),
     'L0_gnn_bn_g': (1.0, 0.2),
     'L0_gnn_bn_b': (0.0, 2.0),
     'L0_gnn_bn_mean': (0.0, 0.8),
     'L0_gnn_bn_var': (1.0, 0.2),
     'L0_gnn_b2': (0.0, 0.8),
     'L0_gnn_ln_g': (1.0, 0.2),
     'L0_gnn_ln_b': (0.0, 0.1)}
    factors = {}
    for name, (base, spread) in spreads.items():
        noise = np.random.default_rng([zlib.crc32(name.encode()), seed]).standard_normal(out[name].shape)
        drawn = base * np.exp(spread * noise) if base else spread * noise
        out[name] = jnp.asarray(drawn.astype(out[name].dtype))
    for name, factor in factors.items():
        out[name] = (out[name] * factor).astype(out[name].dtype)
    return out
```

```python
import concourse.bass as bass
from concourse import mybir
from contextlib import ExitStack

NODES, FEAT, EDGE_FEAT, LAYERS, EDGES = 3125, 128, 64, 3, 53125
EPS = 1e-5
P = 128
NODE_TILE = 112
TILES_IN_BANK = 4
BANK_NODES = NODE_TILE * TILES_IN_BANK
BANK_COLS = 512
WINDOW = BANK_COLS - BANK_NODES
BANKS = -(-NODES // BANK_NODES)
NODE_TILES = BANKS * TILES_IN_BANK
NODES_PAD = BANKS * BANK_NODES
QUAD = 4
SLOTS = 8
BLOCK_QUADS = 4
BLOCK_TILES = QUAD * BLOCK_QUADS
BODY_BLOCKS = SLOTS // BLOCK_QUADS
BODY_TILES = QUAD * SLOTS
BODIES = -(-EDGES // (P * BODY_TILES))
EDGE_TILES = BODIES * BODY_TILES
EDGES_PAD = EDGE_TILES * P
QUADS = EDGE_TILES // QUAD
BLOCKS = EDGE_TILES // BLOCK_TILES
VECS = 6
FORCE_GENERAL = False


def build(nc, x, attr, src, dst, dst_first, edge_w, vecs, w1, w2, b2, ln_g, ln_b, table, out):
    f32, i32 = mybir.dt.float32, mybir.dt.int32
    ALU, ACT, AX = mybir.AluOpType, mybir.ActivationFunctionType, mybir.AxisListType

    with ExitStack() as ctx:
        def sb(name, shape, dt=f32):
            return ctx.enter_context(nc.sbuf_tensor(name, shape, dt))

        def sem(name):
            return ctx.enter_context(nc.semaphore(name))

        x_in = sb("x_in", [NODE_TILE, NODE_TILES, FEAT])
        x_cur = sb("x_cur", [NODE_TILE, NODE_TILES, FEAT])
        zT = sb("zT", [P, BANKS, BANK_COLS])
        hT = sb("hT", [P, BANKS, BANK_NODES])
        norm = sb("norm", [NODE_TILE, NODE_TILES, FEAT])
        stats = sb("stats", [NODE_TILE, NODE_TILES, 6])
        mean_var = sb("mean_var", [NODE_TILE, NODE_TILES, 2])
        std = sb("std", [NODE_TILE, NODE_TILES])
        rstd = sb("rstd", [NODE_TILE, NODE_TILES])
        eps_col = sb("eps_col", [P, 1])
        we = sb("we", [EDGE_FEAT + 1, LAYERS, FEAT])
        w1_all = sb("w1_all", [P, LAYERS, FEAT])
        w1_cur = sb("w1_cur", [P, FEAT])
        w2_all = sb("w2_all", [P, LAYERS, FEAT])
        b2_row = sb("b2_row", [1, LAYERS, FEAT])
        vec = sb("vec", [P, LAYERS, VECS])
        bn_scale = sb("bn_scale", [P, LAYERS])
        bn_bias = sb("bn_bias", [P, LAYERS])
        bn_tmp = sb("bn_tmp", [P, LAYERS])
        eps1 = sb("eps1", [P, LAYERS])
        g_rows = sb("g_rows", [NODE_TILE, FEAT])
        b_rows = sb("b_rows", [NODE_TILE, FEAT])
        ones = sb("ones", [P, P])
        zeros = sb("zeros", [P, WINDOW])
        ident = sb("ident", [NODE_TILE, NODE_TILE])
        ident_eps = sb("ident_eps", [NODE_TILE, LAYERS, NODE_TILE])
        attr_t = sb("attr_t", [EDGE_FEAT + 1, BODY_BLOCKS, BLOCK_TILES * P])
        src_t = sb("src_t", [P, BODY_BLOCKS, BLOCK_TILES], i32)
        rows = sb("rows", [P, SLOTS, QUAD, FEAT])
        pre = sb("pre", [P, 2, QUAD * FEAT])
        msg = sb("msg", [P, 2, QUAD * FEAT])
        onehot = sb("onehot", [P, 2, QUAD, WINDOW])
        onehot_all = sb("onehot_all", [P, BANKS, BANK_COLS])
        iota_i = sb("iota_i", [P, BANKS, BANK_COLS], i32)
        iota_all = sb("iota_all", [P, BANKS, BANK_COLS])
        iota_win = sb("iota_win", [P, WINDOW])
        dst_i = sb("dst_i", [P, EDGE_TILES], i32)
        first_i = sb("first_i", [P, EDGE_TILES], i32)
        dst_f = sb("dst_f", [P, EDGE_TILES])
        first_f = sb("first_f", [P, EDGE_TILES])
        dst_rel = sb("dst_rel", [P, EDGE_TILES])
        col_f = sb("col_f", [1, EDGE_TILES])
        col_tmp = sb("col_tmp", [1, EDGE_TILES])
        col_i = sb("col_i", [1, EDGE_TILES], i32)
        spread = sb("spread", [P, 4])
        flag = sb("flag", [1, 1], i32)

        z_ps = ctx.enter_context(nc.psum_tensor("z_ps", [P, BANKS * BANK_COLS], f32))
        e_ps = ctx.enter_context(nc.psum_tensor("e_ps", [P, QUAD * FEAT], f32))

        x_loaded = sem("x_loaded")
        edges_loaded = sem("edges_loaded")
        weights_loaded = sem("weights_loaded")
        attr_loaded = [sem(f"attr_loaded{n}") for n in range(BODY_BLOCKS)]
        src_loaded = [sem(f"src_loaded{n}") for n in range(BODY_BLOCKS)]
        consts = sem("consts")
        iota_made = sem("iota_made")
        spread_ready = sem("spread_ready")
        spread_sum = sem("spread_sum")
        tables_ready = sem("tables_ready")
        gathered = [sem(f"gathered{n}") for n in range(SLOTS)]
        e_ready = sem("e_ready")
        pre_ready = sem("pre_ready")
        msg_ready = sem("msg_ready")
        onehot_ready = sem("onehot_ready")
        all_ready = sem("all_ready")
        all_used = sem("all_used")
        scattered = sem("scattered")
        w1_ready = sem("w1_ready")
        z_copied = sem("z_copied")
        z_ready = sem("z_ready")
        h_ready = sem("h_ready")
        hT_ready = sem("hT_ready")
        y_ready = sem("y_ready")
        bn_std_ready = sem("bn_std_ready")
        consts_v = sem("consts_v")
        var_ready = sem("var_ready")
        std_ready = sem("std_ready")
        norm_ready = sem("norm_ready")
        x_ready = sem("x_ready")
        table_ready = sem("table_ready")
        dve_step = sem("dve_step")
        out_ready = sem("out_ready")
        out_stored = sem("out_stored")

        block = ctx.enter_context(nc.Block())

        waits_passed = {name: sem(f"waits_passed_{name}") for name in ("pool", "act", "dve", "pe")}

        def wait_alone(eng, name, semaphore, value):
            eng.wait_ge(semaphore, value)
            eng.sem_inc(waits_passed[name], 1)

        def bank(b, n=BANK_COLS, parts=P):
            return z_ps[0:parts, b * BANK_COLS:b * BANK_COLS + n]

        @block.sync
        def _(sp):
            sp.dma_start(dst_i[:, :], dst).then_inc(edges_loaded, 16)
            sp.dma_start(first_i[:, :], dst_first).then_inc(edges_loaded, 16)

            def load_block(l, i, n):
                g = l * BLOCKS + i * BODY_BLOCKS + n
                b = i * BODY_BLOCKS + n
                sp.wait_ge(pre_ready, g * BLOCK_QUADS + BLOCK_QUADS)
                sp.dma_start(src_t[:, n, :], src[bass.ds(b * P, P), :]).then_inc(src_loaded[n], 16)
                sp.wait_ge(e_ready, g * BLOCK_QUADS + BLOCK_QUADS)
                sp.dma_start(attr_t[0:EDGE_FEAT, n, :],
                             attr[bass.ds(b * EDGE_FEAT, EDGE_FEAT), :]).then_inc(attr_loaded[n], 16)

            with sp.Fori(0, LAYERS) as l:
                with sp.Fori(0, BODIES) as i:
                    for n in range(BODY_BLOCKS):
                        load_block(l, i, n)

            for b in range(BANKS):
                sp.wait_ge(out_ready, b + 1)
                sp.dma_start(out[b * BANK_NODES:(b + 1) * BANK_NODES, :].rearrange("(t p) d -> p t d", p=NODE_TILE),
                             norm[:, b * TILES_IN_BANK:(b + 1) * TILES_IN_BANK, :]).then_inc(out_stored, 16)
            sp.wait_ge(out_stored, 16 * BANKS)
            sp.wait_ge(table_ready, 16 * BANKS * LAYERS)

        @block.gpsimd
        def _(pool):
            def gather_layer(l, source):
                with pool.Fori(0, BODIES) as i:
                    for k in range(SLOTS):
                        n = k // BLOCK_QUADS
                        if k % BLOCK_QUADS == 0:
                            pool.wait_ge(src_loaded[n], (i + 1 + l * BODIES) * 16)
                        wait_alone(pool, "pool", pre_ready, l * QUADS + i * SLOTS + k + 1)
                        for j in range(QUAD):
                            c = (k % BLOCK_QUADS) * QUAD + j
                            pool.indirect_dma_start(
                                rows[:, k, j, :], None, source,
                                bass.IndirectOffsetOnAxis(ap=src_t[:, n, c:c + 1], axis=0),
                            ).then_inc(gathered[k], 16)

            nc.gpsimd.iota(iota_i[:, :, :], pattern=[[BANK_NODES, BANKS], [1, BANK_COLS]], base=0,
                           channel_multiplier=0).then_inc(iota_made, 1)
            nc.gpsimd.memset(ident[:, :], 0.0).then_inc(consts, 1)
            pool.wait_ge(consts, 1)
            nc.gpsimd.affine_select(out=ident[:, :], in_=ident[:, :], compare_op=ALU.not_equal, fill=1.0,
                                    base=0, pattern=[[-1, NODE_TILE]], channel_multiplier=1).then_inc(iota_made, 1)
            gather_layer(0, x)
            with pool.Fori(1, LAYERS) as l:
                wait_alone(pool, "pool", table_ready, l * (16 * BANKS))
                gather_layer(l, table)

        def deviation(act, l, b):
            t = slice(b * TILES_IN_BANK, (b + 1) * TILES_IN_BANK)
            act.wait_ge(var_ready, l * BANKS + (b + 1))
            nc.scalar.activation(std[:, t], mean_var[:, t, 1], ACT.Sqrt,
                                 bias=eps_col[0:NODE_TILE, :]).then_inc(std_ready, 1)

        def new_features(act, l, b):
            t = slice(b * TILES_IN_BANK, (b + 1) * TILES_IN_BANK)
            act.wait_ge(norm_ready, l * BANKS + b + 1)
            nc.scalar.activation(x_cur[:, t, :], norm[:, t, :], ACT.Relu).then_inc(x_ready, 1)

        def store_table(act, l, b):
            t = slice(b * TILES_IN_BANK, (b + 1) * TILES_IN_BANK)
            act.wait_ge(x_ready, l * BANKS + (BANKS + b + 1))
            act.dma_start(table[b * BANK_NODES:(b + 1) * BANK_NODES, :].rearrange("(t p) d -> p t d", p=NODE_TILE),
                          x_cur[:, t, :]).then_inc(table_ready, 16)

        @block.scalar
        def _(act):
            act.dma_start(x_in[:, :, :], x.rearrange("(t p) d -> p t d", p=NODE_TILE)).then_inc(x_loaded, 16)
            act.dma_start(we[:, :, :], edge_w).then_inc(weights_loaded, 16)
            act.dma_start(vec[:, :, :], vecs).then_inc(weights_loaded, 16)
            act.dma_start(w1_all[:, :, :], w1).then_inc(weights_loaded, 16)
            act.dma_start(w2_all[:, :, :], w2).then_inc(weights_loaded, 16)
            act.dma_start(b2_row[:, :, :], b2).then_inc(weights_loaded, 16)
            act.dma_start(g_rows[:, :], ln_g).then_inc(weights_loaded, 16)
            act.dma_start(b_rows[:, :], ln_b).then_inc(weights_loaded, 16)
            act.wait_ge(x_loaded, 16)
            for b in range(BANKS):
                t = slice(b * TILES_IN_BANK, (b + 1) * TILES_IN_BANK)
                nc.scalar.activation(x_cur[:, t, :], x_in[:, t, :], ACT.Copy).then_inc(x_ready, 1)
            act.wait_ge(weights_loaded, 16 * 7)
            act.wait_ge(consts_v, 1)
            nc.scalar.activation(bn_tmp[:, :], vec[:, :, 4], ACT.Sqrt, bias=eps_col[:, :]).then_inc(bn_std_ready, 1)

            with act.Fori(0, LAYERS) as l:
                with act.Fori(0, BODIES) as i:
                    for k in range(SLOTS):
                        act.wait_ge(pre_ready, l * QUADS + i * SLOTS + (SLOTS + k + 1))
                        nc.scalar.activation(msg[:, k % 2, :], pre[:, k % 2, :], ACT.Relu).then_inc(msg_ready, 1)
                act.wait_ge(scattered, (l + 1) * QUADS)
                for b in range(BANKS):
                    nc.scalar.activation(zT[:, b, :], bank(b), ACT.Copy).then_inc(z_copied, 1)
                    if b == 0:
                        nc.scalar.activation(w1_cur[:, :], w1_all[:, bass.ds(l, 1), :].rearrange("p a d -> p (a d)"),
                                             ACT.Copy).then_inc(w1_ready, 1)
                for n in range(BANKS + 4):
                    if n < BANKS:
                        wait_alone(act, "act", h_ready, l * BANKS + n + 1)
                        nc.scalar.activation(hT[:, n, :], bank(n, BANK_NODES), ACT.Relu,
                                             scale=bn_scale[:, bass.ds(l, 1)],
                                             bias=bn_bias[:, bass.ds(l, 1)]).then_inc(hT_ready, 1)
                    if 2 <= n < BANKS + 2:
                        deviation(act, l, n - 2)
                    if 3 <= n < BANKS + 3:
                        new_features(act, l, n - 3)
                    if 4 <= n:
                        store_table(act, l, n - 4)
            for b in range(BANKS):
                deviation(act, LAYERS, b)

        @block.vector
        def _(dve):
            done = [0]

            def step(ins):
                done[0] += 1
                ins.then_inc(dve_step, 1)
                dve.wait_ge(dve_step, done[0])

            nc.vector.memset(attr_t[EDGE_FEAT:EDGE_FEAT + 1, :, :], 1.0)
            nc.vector.memset(ones[:, :], 1.0)
            step(nc.vector.memset(zeros[:, :], 0.0))
            nc.vector.memset(eps_col[:, :], EPS).then_inc(consts_v, 1)
            dve.sem_inc(e_ready, SLOTS)
            dve.sem_inc(pre_ready, SLOTS)

            dve.wait_ge(edges_loaded, 32)
            nc.vector.tensor_copy(dst_f[:, :], dst_i[:, :])
            step(nc.vector.tensor_copy(first_f[:, :], first_i[:, :]))
            step(nc.vector.tensor_tensor(dst_rel[:, :], dst_f[:, :], first_f[:, :], ALU.subtract))
            nc.vector.tensor_reduce(spread[:, 0:1], dst_rel[:, :], AX.X, ALU.max)
            step(nc.vector.tensor_reduce(spread[:, 1:2], dst_rel[:, :], AX.X, ALU.min))
            nc.vector.tensor_scalar(spread[:, 2:3], spread[:, 0:1], -1.0 if FORCE_GENERAL else float(WINDOW), None, ALU.is_ge)
            step(nc.vector.tensor_scalar(spread[:, 3:4], spread[:, 1:2], 0.0, None, ALU.is_lt))
            nc.vector.tensor_tensor(spread[:, 0:1], spread[:, 2:3], spread[:, 3:4], ALU.add).then_inc(spread_ready, 1)
            step(nc.vector.tensor_copy(col_f[:, :], first_f[0:1, :]))
            for b in range(1, BANKS):
                step(nc.vector.tensor_scalar(col_tmp[:, :], first_f[0:1, :], float(b * BANK_NODES), float(WINDOW),
                                             ALU.is_ge, ALU.mult))
                step(nc.vector.tensor_tensor(col_f[:, :], col_f[:, :], col_tmp[:, :], ALU.add))
            step(nc.vector.tensor_copy(col_i[:, :], col_f[:, :]))

            dve.wait_ge(iota_made, 2)
            step(nc.vector.tensor_copy(iota_all[:, :, :], iota_i[:, :, :]))
            step(nc.vector.tensor_copy(iota_win[:, :], iota_all[:, 0, 0:WINDOW]))
            step(nc.vector.memset(iota_all[:, :, BANK_NODES:BANK_COLS], -1.0))

            dve.wait_ge(weights_loaded, 16 * 7)
            dve.wait_ge(bn_std_ready, 1)
            step(nc.vector.reciprocal(bn_scale[:, :], bn_tmp[:, :]))
            step(nc.vector.tensor_tensor(bn_scale[:, :], bn_scale[:, :], vec[:, :, 1], ALU.mult))
            step(nc.vector.tensor_tensor(bn_tmp[:, :], vec[:, :, 0], vec[:, :, 3], ALU.subtract))
            step(nc.vector.tensor_tensor(bn_bias[:, :], bn_tmp[:, :], bn_scale[:, :], ALU.mult))
            step(nc.vector.tensor_tensor(bn_bias[:, :], bn_bias[:, :], vec[:, :, 2], ALU.add))
            step(nc.vector.tensor_scalar(eps1[:, :], vec[:, :, 5], 1.0, None, ALU.add))
            for l in range(LAYERS):
                step(nc.vector.tensor_scalar(ident_eps[:, l, :], ident[:, :], eps1[0:NODE_TILE, l:l + 1], None, ALU.mult))
            dve.wait_ge(spread_sum, 1)
            step(nc.vector.tensor_copy(flag[:, :], e_ps[0:1, 0:1]))
            dve.sem_inc(tables_ready, 1)

            def edges(l, wide):
                with dve.Fori(0, BODIES) as i:
                    for k in range(SLOTS):
                        q = l * QUADS + i * SLOTS + k
                        tile = i * BODY_TILES + k * QUAD
                        dve.wait_ge(e_ready, q + (SLOTS + 1))
                        dve.wait_ge(gathered[k], (i + 1 + l * BODIES) * (16 * QUAD))
                        nc.vector.tensor_tensor(pre[:, k % 2, :], e_ps[:, :],
                                                rows[:, k, :, :].rearrange("p j d -> p (j d)"),
                                                ALU.add).then_inc(pre_ready, 1)
                        if not wide:
                            nc.vector.tensor_tensor(
                                onehot[:, k % 2, :, :],
                                iota_win[:, :].unsqueeze(1).to_broadcast([P, QUAD, WINDOW]),
                                dst_rel[:, bass.ds(tile, QUAD)].unsqueeze(2).to_broadcast([P, QUAD, WINDOW]),
                                ALU.is_equal).then_inc(onehot_ready, 1)
                        else:
                            for j in range(QUAD):
                                dve.wait_ge(all_used, q * QUAD + (j + 1))
                                nc.vector.tensor_scalar(
                                    onehot_all[:, :, :], iota_all[:, :, :], dst_f[:, bass.ds(tile + j, 1)], None,
                                    ALU.is_equal).then_inc(all_ready, 1)

            general = dve.value_load(flag[0:1, 0:1])
            dve.sem_inc(all_used, 1)
            per_layer = BANKS * 2
            before = done[0]

            with dve.Fori(0, LAYERS) as l:
                with dve.If(general == 0):
                    edges(l, False)
                with dve.Else():
                    edges(l, True)
                for b in range(1, BANKS):
                    dve.wait_ge(z_copied, l * BANKS + b + 1)
                    nc.vector.tensor_tensor(zT[:, b, 0:WINDOW], zT[:, b, 0:WINDOW], zT[:, b - 1, BANK_NODES:],
                                            ALU.add).then_inc(z_ready, 1)
                n = 0
                for b in range(BANKS):
                    t0 = b * TILES_IN_BANK
                    tiles = range(t0, t0 + TILES_IN_BANK)
                    y = bank(b, parts=NODE_TILE).rearrange("p (t d) -> p t d", t=TILES_IN_BANK)
                    dve.wait_ge(y_ready, l * BANKS + b + 1)
                    for t in tiles:
                        ins = nc.vector.bn_stats(stats[:, t, :], y[:, t - t0, :])
                    ins.then_inc(dve_step, 1)
                    n += 1
                    wait_alone(dve, "dve", dve_step, l * per_layer + (before + n))
                    for t in tiles:
                        ins = nc.vector.bn_aggr(mean_var[:, t, :], stats[:, t, :])
                    ins.then_inc(var_ready, 1)
                    dve.wait_ge(var_ready, l * BANKS + b + 1)
                    for t in tiles:
                        nc.vector.scalar_tensor_tensor(
                            norm[:, t, :], y[:, t - t0, :], mean_var[:, t, 0:1], g_rows[:, :],
                            ALU.subtract, ALU.mult)
                    dve.wait_ge(std_ready, l * BANKS + b + 1)
                    nc.vector.reciprocal(rstd[:, t0:t0 + TILES_IN_BANK],
                                         std[:, t0:t0 + TILES_IN_BANK]).then_inc(dve_step, 1)
                    n += 1
                    dve.wait_ge(dve_step, l * per_layer + (before + n))
                    for t in tiles:
                        ins = nc.vector.scalar_tensor_tensor(
                            norm[:, t, :], norm[:, t, :], rstd[:, t:t + 1], b_rows[:, :], ALU.mult, ALU.add)
                    ins.then_inc(norm_ready, 1)
            assert n == per_layer
            done[0] = before + LAYERS * per_layer

            def final_stats(b):
                ts = slice(b * TILES_IN_BANK, (b + 1) * TILES_IN_BANK)
                dve.wait_ge(x_ready, LAYERS * BANKS + b + 1)
                step(nc.vector.tensor_tensor(x_in[:, ts, :], x_in[:, ts, :], x_cur[:, ts, :], ALU.add))
                for t in range(ts.start, ts.stop):
                    ins = nc.vector.bn_stats(stats[:, t, :], x_in[:, t, :])
                step(ins)
                for t in range(ts.start, ts.stop):
                    ins = nc.vector.bn_aggr(mean_var[:, t, :], stats[:, t, :])
                ins.then_inc(var_ready, 1)

            def final_norm(b):
                ts = slice(b * TILES_IN_BANK, (b + 1) * TILES_IN_BANK)
                dve.wait_ge(std_ready, LAYERS * BANKS + b + 1)
                step(nc.vector.reciprocal(rstd[:, ts], std[:, ts]))
                for t in range(ts.start, ts.stop):
                    ins = nc.vector.tensor_scalar(norm[:, t, :], x_in[:, t, :], mean_var[:, t, 0:1], rstd[:, t:t + 1],
                                                  ALU.subtract, ALU.mult)
                ins.then_inc(out_ready, 1)

            final_stats(0)
            for b in range(1, BANKS):
                final_stats(b)
                final_norm(b - 1)
            final_norm(BANKS - 1)

        @block.tensor
        def _(pe):
            pe.wait_ge(spread_ready, 1)
            nc.tensor.matmul(e_ps[0:1, 0:1], spread[:, 0:1], ones[:, 0:1], start=True, stop=True).then_inc(spread_sum, 1)
            pe.wait_ge(tables_ready, 1)
            general = pe.value_load(flag[0:1, 0:1])

            def edge_terms(l, i, k):
                n = k // BLOCK_QUADS
                if k % BLOCK_QUADS == 0:
                    pe.wait_ge(attr_loaded[n], (i + 1 + l * BODIES) * 16)
                if k >= 1:
                    pe.wait_ge(pre_ready, l * QUADS + i * SLOTS + (SLOTS + k))
                for j in range(QUAD):
                    c = ((k % BLOCK_QUADS) * QUAD + j) * P
                    ins = nc.tensor.matmul(
                        e_ps[:, j * FEAT:(j + 1) * FEAT], attr_t[:, n, c:c + P],
                        we[:, bass.ds(l, 1), :].rearrange("p a d -> p (a d)"), start=True, stop=True)
                ins.then_inc(e_ready, 1)

            def scatter(l, i, k, wide):
                q = l * QUADS + i * SLOTS + k
                tile = i * BODY_TILES + k * QUAD
                if not wide:
                    cols = [pe.value_load(col_i[0:1, bass.ds(tile + j, 1)], min_val=0,
                                          max_val=BANKS * BANK_COLS - WINDOW) for j in range(QUAD)]
                    pe.wait_ge(onehot_ready, q + 1)
                pe.wait_ge(msg_ready, q + 1)
                for j in range(QUAD):
                    m = msg[:, k % 2, j * FEAT:(j + 1) * FEAT]
                    if not wide:
                        ins = nc.tensor.matmul(z_ps[:, bass.ds(cols[j], WINDOW)], m, onehot[:, k % 2, j, :],
                                               start=False, stop=False, skip_group_check=True)
                    else:
                        pe.wait_ge(all_ready, q * QUAD + (j + 1))
                        for b in range(BANKS):
                            ins = nc.tensor.matmul(bank(b), m, onehot_all[:, b, :],
                                                   start=False, stop=False, skip_group_check=True)
                        if j < QUAD - 1:
                            ins.then_inc(all_used, 1)
                ins.then_inc(scattered, 1)
                if wide:
                    pe.wait_ge(scattered, q + 1)
                    pe.sem_inc(all_used, 1)

            def edges(l, wide):
                with pe.Fori(0, BODIES) as i:
                    edge_terms(l, i, 0)
                    for k in range(1, SLOTS):
                        edge_terms(l, i, k)
                        scatter(l, i, k - 1, wide)
                    scatter(l, i, SLOTS - 1, wide)

            with pe.Fori(0, LAYERS) as l:
                for b in range(BANKS):
                    pe.wait_ge(x_ready, l * BANKS + b + 1)
                    nc.tensor.matmul(bank(b)[:, BANK_NODES:], ones[0:1, :], zeros[0:1, :],
                                     start=True, stop=False, skip_group_check=True)
                    for j in range(TILES_IN_BANK):
                        nc.tensor.matmul(bank(b)[:, j * NODE_TILE:(j + 1) * NODE_TILE],
                                         x_cur[:, b * TILES_IN_BANK + j, :],
                                         ident_eps[:, bass.ds(l, 1), :].rearrange("p a d -> p (a d)"),
                                         start=False, stop=False, skip_group_check=True)
                with pe.If(general == 0):
                    edges(l, False)
                with pe.Else():
                    edges(l, True)

                def hidden(b):
                    if b == 0:
                        pe.wait_ge(w1_ready, l + 1)
                        pe.wait_ge(z_copied, l * BANKS + 1)
                    else:
                        pe.wait_ge(z_ready, l * (BANKS - 1) + b)
                    nc.tensor.matmul(bank(b, BANK_NODES), w1_cur[:, :], zT[:, b, 0:BANK_NODES],
                                     start=True, stop=True, skip_group_check=True).then_inc(h_ready, 1)

                def output(b):
                    wait_alone(pe, "pe", hT_ready, l * BANKS + b + 1)
                    y = bank(b, parts=NODE_TILE)
                    nc.tensor.matmul(y, ones[0:1, 0:NODE_TILE],
                                     b2_row[:, bass.ds(l, 1), :].to_broadcast([1, TILES_IN_BANK, FEAT]),
                                     start=True, stop=False, skip_group_check=True)
                    for j in range(TILES_IN_BANK):
                        ins = nc.tensor.matmul(y[:, j * FEAT:(j + 1) * FEAT],
                                               hT[:, b, j * NODE_TILE:(j + 1) * NODE_TILE],
                                               w2_all[:, bass.ds(l, 1), :].rearrange("p a d -> p (a d)"),
                                               start=False, stop=j == TILES_IN_BANK - 1, skip_group_check=True)
                    ins.then_inc(y_ready, 1)

                hidden(0)
                for b in range(1, BANKS):
                    hidden(b)
                    output(b - 1)
                output(BANKS - 1)


def kernel(**inputs):
    import numpy as np
    import concourse.bacc as bacc
    from concourse.bass_utils import run_bass_kernel_spmd

    def pad(a, n, value=0):
        a = np.asarray(a)
        filled = np.full((n,) + a.shape[1:], value, a.dtype)
        filled[:a.shape[0]] = a
        return filled

    def rows(name, n):
        a = np.asarray(inputs[name])
        return np.ascontiguousarray(np.broadcast_to(a[None], (n,) + a.shape))

    dst = pad(inputs["dst"], EDGES_PAD, NODES).reshape(EDGE_TILES, P)
    src = pad(inputs["src"], EDGES_PAD)
    attr = pad(inputs["edge_attr_64"], EDGES_PAD)
    eps = np.broadcast_to(np.asarray(inputs["L0_gnn_eps"])[:, None], (LAYERS, FEAT))
    columns = [inputs["L0_gnn_" + k] for k in ("b1", "bn_g", "bn_b", "bn_mean", "bn_var")] + [eps]
    arrays = {
        "x": pad(inputs["x"], NODES_PAD),
        "attr": attr.reshape(BLOCKS, BLOCK_TILES * P, EDGE_FEAT).transpose(0, 2, 1).reshape(BLOCKS * EDGE_FEAT, -1),
        "src": src.reshape(BLOCKS, BLOCK_TILES, P).transpose(0, 2, 1).reshape(BLOCKS * P, BLOCK_TILES),
        "dst": dst.T,
        "dst_first": np.broadcast_to(dst[:, 0], (P, EDGE_TILES)),
        "edge_w": np.concatenate([np.asarray(inputs["L0_gnn_edge_W"]),
                                  np.asarray(inputs["L0_gnn_edge_b"])[:, None]], 1).transpose(1, 0, 2),
        "vecs": np.stack([np.asarray(c) for c in columns], -1).transpose(1, 0, 2),
        "w1": np.asarray(inputs["L0_gnn_W1"]).transpose(1, 0, 2),
        "w2": np.asarray(inputs["L0_gnn_W2"]).transpose(1, 0, 2),
        "b2": np.asarray(inputs["L0_gnn_b2"])[None],
        "ln_g": rows("L0_gnn_ln_g", NODE_TILE),
        "ln_b": rows("L0_gnn_ln_b", NODE_TILE),
    }
    arrays = {k + "_dram": np.ascontiguousarray(v) for k, v in arrays.items()}
    nc = bacc.Bacc("TRN2", target_bir_lowering=False, num_devices=1)
    args = [nc.dram_tensor(k, v.shape, mybir.dt.from_np(v.dtype), kind="ExternalInput").ap() for k, v in arrays.items()]
    table = nc.dram_tensor("table_dram", (NODES_PAD, FEAT), mybir.dt.float32, kind="Internal").ap()
    out = nc.dram_tensor("out_dram", (NODES_PAD, FEAT), mybir.dt.float32, kind="ExternalOutput").ap()
    build(nc, *args, table, out)
    result = run_bass_kernel_spmd(nc, [arrays], core_ids=[0])
    return result.results[0]["out_dram"][:NODES]
```

```python
import concourse.bass as bass
from concourse import mybir
from contextlib import ExitStack

NODES, FEAT, EDGE_FEAT, LAYERS, EDGES = 3125, 128, 64, 3, 53125
EPS = 1e-5
P = 128
BANK_COLS = 512
QUAD = 4
SLOTS = 8
BLOCK_QUADS = 4
BLOCK_TILES = QUAD * BLOCK_QUADS
BLOCKS_IN_BODY = SLOTS // BLOCK_QUADS
BODY_TILES = QUAD * SLOTS
BODIES = -(-EDGES // (P * BODY_TILES))
EDGE_TILES = BODIES * BODY_TILES
EDGES_PAD = EDGE_TILES * P
QUADS = EDGE_TILES // QUAD
BLOCKS = EDGE_TILES // BLOCK_TILES
NODE_TILE = -(-NODES // BLOCKS)
NODE_TILES = BLOCKS
NODES_PAD = NODE_TILES * NODE_TILE
WINDOW = 64
OVERLAP = BANK_COLS - NODE_TILE
GROUP = BANK_COLS // FEAT
GROUPS = -(-NODE_TILES // GROUP)
GROUP_COLS = GROUP * NODE_TILE
B2_PARTS = 3
BUFFERS = 4
AHEAD = BUFFERS - 1
VECS = 6


def turn(l, i, k):
    return (l * BODIES + i) * SLOTS + (k + 1)


def node(l, t):
    return l * NODE_TILES + t + 1


def build(nc, x, attr, src, dst, dst_first, edge_w, vecs, w1, w2, b2, ln_g, ln_b, tables, out):
    f32, i32, bf16 = mybir.dt.float32, mybir.dt.int32, mybir.dt.bfloat16
    ALU, ACT, AX = mybir.AluOpType, mybir.ActivationFunctionType, mybir.AxisListType
    NT = NODE_TILE

    with ExitStack() as ctx:
        def sb(name, shape, dt=f32):
            return ctx.enter_context(nc.sbuf_tensor(name, shape, dt))

        def sem(name):
            return ctx.enter_context(nc.semaphore(name))

        x_in = sb("x_in", [NT, NODE_TILES, FEAT])
        x_cur = sb("x_cur", [NT, NODE_TILES, FEAT])
        wide = sb("wide", [P, NODE_TILES, FEAT])
        result = wide[0:NT, :, :]
        z_sum = sb("z_sum", [P, (NODE_TILES - 1) * NT + BANK_COLS])
        x_eps = sb("x_eps", [NT, 2, FEAT])
        zT = sb("zT", [P, 2, NT])
        hT = sb("hT", [P, 2, NT])
        norm = sb("norm", [NT, 2, FEAT])
        stats = sb("stats", [NT, NODE_TILES, 6])
        mean_var = sb("mean_var", [NT, NODE_TILES, 2])
        std = sb("std", [NT, NODE_TILES])
        rstd = sb("rstd", [NT, NODE_TILES])
        zT_all = z_sum[:, 0:NODES_PAD]
        hT_all = wide[:, :, :].rearrange("p t d -> p (t d)")[:, 0:NODES_PAD]
        we = sb("we", [EDGE_FEAT + 1, LAYERS, FEAT])
        w1_all = sb("w1_all", [P, LAYERS, FEAT])
        w1_cur = sb("w1_cur", [P, FEAT])
        w2_all = sb("w2_all", [P, LAYERS, FEAT])
        b2_rows = sb("b2_rows", [B2_PARTS, LAYERS, FEAT])
        b2_rest = sb("b2_rest", [B2_PARTS, LAYERS, FEAT])
        b2_part = sb("b2_part", [B2_PARTS, LAYERS, FEAT], bf16)
        b2_split = sb("b2_split", [B2_PARTS, LAYERS, FEAT], bf16)
        ones_b = sb("ones_b", [B2_PARTS, P], bf16)
        zeros_b = sb("zeros_b", [1, BANK_COLS], bf16)
        vec = sb("vec", [P, LAYERS, VECS])
        bn_std = sb("bn_std", [P, LAYERS])
        bn_scale = sb("bn_scale", [P, LAYERS])
        bn_bias = sb("bn_bias", [P, LAYERS])
        bn_tmp = sb("bn_tmp", [P, LAYERS])
        eps1 = sb("eps1", [P, LAYERS])
        eps_col = sb("eps_col", [P, 1])
        g_rows = sb("g_rows", [P, FEAT])
        b_rows = sb("b_rows", [P, FEAT])
        ident = sb("ident", [P, P])
        attr_t = sb("attr_t", [EDGE_FEAT + 1, BLOCKS_IN_BODY, BLOCK_TILES * P])
        src_t = sb("src_t", [P, BLOCKS_IN_BODY, BLOCK_TILES], i32)
        rows = sb("rows", [P, SLOTS, QUAD, FEAT])
        pre = sb("pre", [P, BUFFERS, QUAD * FEAT])
        msg = sb("msg", [P, BUFFERS, QUAD * FEAT])
        onehot = sb("onehot", [P, BUFFERS, QUAD, WINDOW])
        onehot_all = sb("onehot_all", [P, GROUP_COLS])
        iota_i = sb("iota_i", [P, BANK_COLS], i32)
        iota_f = sb("iota_f", [P, BANK_COLS])
        dst_i = sb("dst_i", [P, EDGE_TILES], i32)
        first_i = sb("first_i", [P, EDGE_TILES], i32)
        dst_f = sb("dst_f", [P, EDGE_TILES])
        first_f = sb("first_f", [P, EDGE_TILES])
        dst_rel = sb("dst_rel", [P, EDGE_TILES])
        base_i = sb("base_i", [P, QUADS], i32)
        col_f = sb("col_f", [P, QUADS])
        col_i = sb("col_i", [P, QUADS], i32)
        ends = sb("ends", [P, 4])
        misfits = sb("misfits", [P, 4])
        misfit = sb("misfit", [P, 1])
        ones = sb("ones", [P, 1])
        flag = sb("flag", [1, 1], i32)

        ps = ctx.enter_context(nc.psum_tensor("ps", [P, 8 * BANK_COLS], f32))

        def bank(b, n=BANK_COLS):
            return ps[:, b * BANK_COLS:b * BANK_COLS + n]

        def z_bank(h):
            return bank(BUFFERS + h)

        def zh_cols(h, second):
            return bank(6)[:, second * 256 + h * P:second * 256 + h * P + NT]

        def y_cols(h):
            return ps[0:NT, 7 * BANK_COLS + h * FEAT:7 * BANK_COLS + (h + 1) * FEAT]

        x_loaded = sem("x_loaded")
        edges_loaded = sem("edges_loaded")
        weights_loaded = sem("weights_loaded")
        attr_loaded = [sem(f"attr_loaded{n}") for n in range(BLOCKS_IN_BODY)]
        src_loaded = [sem(f"src_loaded{n}") for n in range(BLOCKS_IN_BODY)]
        ident_zero = sem("ident_zero")
        iota_made = sem("iota_made")
        misfit_ready = sem("misfit_ready")
        misfit_sum = sem("misfit_sum")
        flag_ready = sem("flag_ready")
        eps_ready = sem("eps_ready")
        bn_std_ready = sem("bn_std_ready")
        tables_ready = sem("tables_ready")
        gathered = [sem(f"gathered{n}") for n in range(SLOTS)]
        bank_filled = sem("bank_filled")
        bank_taken = sem("bank_taken")
        msg_ready = sem("msg_ready")
        onehot_ready = sem("onehot_ready")
        segment_done = sem("segment_done")
        flushed = sem("flushed")
        w1_ready = sem("w1_ready")
        x_eps_ready = sem("x_eps_ready")
        xT_ready = sem("xT_ready")
        z_ready = sem("z_ready")
        h_ready = sem("h_ready")
        hT_ready = sem("hT_ready")
        y_ready = sem("y_ready")
        stats_ready = sem("stats_ready")
        var_ready = sem("var_ready")
        std_ready = sem("std_ready")
        rstd_ready = sem("rstd_ready")
        norm_ready = sem("norm_ready")
        x_ready = sem("x_ready")
        table_ready = sem("table_ready")
        dve_step = sem("dve_step")
        last_var = sem("last_var")
        last_std = sem("last_std")
        out_ready = sem("out_ready")
        out_stored = sem("out_stored")
        g_filled = sem("g_filled")
        g_taken = sem("g_taken")
        g_msg = sem("g_msg")
        g_hot = sem("g_hot")
        g_used = sem("g_used")
        g_layer = sem("g_layer")
        g_step = sem("g_step")
        waits_passed = {name: sem(f"waits_passed_{name}") for name in ("sp", "pool", "act", "dve", "pe")}

        block = ctx.enter_context(nc.Block())

        def wait_alone(eng, name, semaphore, value):
            eng.wait_ge(semaphore, value)
            eng.sem_inc(waits_passed[name], 1)

        def one(array, l):
            return array[:, bass.ds(l, 1), :].rearrange("p a d -> p (a d)")

        def groups():
            return [slice(g * GROUP, min((g + 1) * GROUP, NODE_TILES)) for g in range(GROUPS)]

        def load_attr(eng, i, n):
            eng.dma_start(attr_t[0:EDGE_FEAT, n, :],
                          attr[bass.ds((i * BLOCKS_IN_BODY + n) * EDGE_FEAT, EDGE_FEAT), :]).then_inc(attr_loaded[n], 16)

        @block.sync
        def _(sp):
            def load_src(i, n):
                sp.dma_start(src_t[:, n, :], src[bass.ds((i * BLOCKS_IN_BODY + n) * P, P), :]).then_inc(src_loaded[n], 16)

            for n in range(BLOCKS_IN_BODY):
                load_src(0, n)
            sp.dma_start(dst_i[:, :], dst).then_inc(edges_loaded, 16)
            sp.dma_start(first_i[:, :], dst_first).then_inc(edges_loaded, 16)
            for n in range(BLOCKS_IN_BODY):
                load_attr(sp, 0, n)
            with sp.Fori(0, LAYERS) as l:
                with sp.Fori(0, BODIES) as i:
                    for n in range(BLOCKS_IN_BODY):
                        for k in range(n * BLOCK_QUADS, (n + 1) * BLOCK_QUADS):
                            wait_alone(sp, "sp", gathered[k], (i + 1 + l * BODIES) * (16 * QUAD))
                        load_src(i + 1, n)

            for semaphore in src_loaded + attr_loaded:
                sp.wait_ge(semaphore, (LAYERS * BODIES + 1) * 16)
            for g, ts in enumerate(groups()):
                sp.wait_ge(out_ready, g + 1)
                sp.dma_start(out[ts.start * NT:ts.stop * NT, :].rearrange("(t p) d -> p t d", p=NT),
                             result[:, ts, :]).then_inc(out_stored, 16)
            sp.wait_ge(out_stored, 16 * GROUPS)

        @block.gpsimd
        def _(pool):
            def gather(source, k):
                for j in range(QUAD):
                    c = (k % BLOCK_QUADS) * QUAD + j
                    pool.indirect_dma_start(
                        rows[:, k, j, :], None, source,
                        bass.IndirectOffsetOnAxis(ap=src_t[:, k // BLOCK_QUADS, c:c + 1], axis=0),
                    ).then_inc(gathered[k], 16)

            def wait_src(l, i, k):
                if k % BLOCK_QUADS == 0:
                    pool.wait_ge(src_loaded[k // BLOCK_QUADS], (i + (1 + l * BODIES)) * 16)

            nc.gpsimd.iota(base_i[:, :], pattern=[[-NT, BLOCKS], [0, BLOCK_QUADS]], base=NT,
                           channel_multiplier=0).then_inc(iota_made, 1)
            nc.gpsimd.iota(iota_i[:, :], pattern=[[1, BANK_COLS]], base=0, channel_multiplier=0).then_inc(iota_made, 1)
            nc.gpsimd.memset(ident[:, :], 0.0).then_inc(ident_zero, 1)
            pool.wait_ge(ident_zero, 1)
            nc.gpsimd.affine_select(out=ident[:, :], in_=ident[:, :], compare_op=ALU.not_equal, fill=1.0,
                                    base=0, pattern=[[-1, P]], channel_multiplier=1).then_inc(iota_made, 1)
            for k in range(SLOTS):
                wait_src(0, 0, k)
                gather(x, k)

            pool.wait_ge(flag_ready, 1)
            general = pool.value_load(flag[0:1, 0:1])
            for l, source in enumerate([x] + tables):
                with pool.If(general == 0):
                    if l >= 1:
                        pool.wait_ge(table_ready, 16 * NODE_TILES * l)
                    with pool.Fori(1 if l == 0 else 0, BODIES) as i:
                        for k in range(SLOTS):
                            wait_src(l, i, k)
                            wait_alone(pool, "pool", bank_taken, i * SLOTS + (l * QUADS + k + 1))
                            gather(source, k)
                with pool.Else():
                    if l >= 1:
                        pool.wait_ge(table_ready, 16 * l)
                    with pool.Fori(1 if l == 0 else 0, BODIES) as i:
                        for k in range(SLOTS):
                            wait_src(l, i, k)
                            wait_alone(pool, "pool", g_taken, i * SLOTS + (l * QUADS + k + 1))
                            gather(source, k)

        @block.scalar
        def _(act):
            act.dma_start(x_in[:, :, :], x[0:NODES_PAD, :].rearrange("(t p) d -> p t d", p=NT)).then_inc(x_loaded, 16)
            for to, of in ((we, edge_w), (vec, vecs), (w1_all, w1), (w2_all, w2), (b2_rows, b2)):
                act.dma_start(to[:, :, :], of).then_inc(weights_loaded, 16)
            for to, of in ((g_rows, ln_g), (b_rows, ln_b)):
                act.dma_start(to[:, :], of).then_inc(weights_loaded, 16)
            act.wait_ge(x_loaded, 16)
            nc.scalar.activation(x_cur[:, :, :], x_in[:, :, :], ACT.Copy).then_inc(x_ready, NODE_TILES)
            act.wait_ge(weights_loaded, 16 * 7)
            act.wait_ge(eps_ready, 1)
            nc.scalar.activation(bn_std[:, :], vec[:, :, 4], ACT.Sqrt, bias=eps_col[:, :]).then_inc(bn_std_ready, 1)
            act.wait_ge(tables_ready, 1)
            general = act.value_load(flag[0:1, 0:1])

            def scaled(l, t, h, upto=None):
                nc.scalar.activation(x_eps[:, h, :], one(x_cur, t), ACT.Identity,
                                     scale=eps1[0:NT, bass.ds(l, 1)]).then_inc(x_eps_ready, 1)

            def hidden(l, t, h, upto=None):
                wait_alone(act, "act", h_ready, node(l, upto or t))
                nc.scalar.activation(hT[:, h, :], zh_cols(h, 1), ACT.Relu, scale=bn_scale[:, bass.ds(l, 1)],
                                     bias=bn_bias[:, bass.ds(l, 1)]).then_inc(hT_ready, 1)

            def deviation(l, t, h, upto=None):
                act.wait_ge(var_ready, node(l, t))
                nc.scalar.activation(std[:, h:h + 1], mean_var[:, h, 1:2], ACT.Sqrt,
                                     bias=eps_col[0:NT, :]).then_inc(std_ready, 1)

            def features(l, t, h, upto=None):
                wait_alone(act, "act", norm_ready, node(l, t))
                nc.scalar.activation(one(x_cur, t), norm[:, h, :], ACT.Relu).then_inc(x_ready, 1)
                wait_alone(act, "act", x_ready, node(l, t) + NODE_TILES)
                for n, table in enumerate(tables):
                    with act.If(l == n):
                        act.dma_start(table[bass.ds(t * NT, NT), :], one(x_cur, t)).then_inc(table_ready, 16)

            def message(l, i, k):
                act.wait_ge(bank_taken, turn(l, i, k) + SLOTS)
                nc.scalar.activation(msg[:, k % BUFFERS, :], pre[:, k % BUFFERS, :], ACT.Relu).then_inc(msg_ready, 1)
                if k % BLOCK_QUADS == BLOCK_QUADS - 1:
                    load_attr(act, i + 1, k // BLOCK_QUADS)

            def body(l, i, nodes):
                t0, t1 = i * 2 - 2, i * 2 - 1
                if nodes:
                    scaled(l, t0, 0)
                message(l, i, 0)
                message(l, i, 1)
                if nodes:
                    hidden(l, t0, 0)
                message(l, i, 2)
                message(l, i, 3)
                if nodes:
                    deviation(l, t0, 0)
                    scaled(l, t1, 1)
                message(l, i, 4)
                if nodes:
                    features(l, t0, 0)
                message(l, i, 5)
                if nodes:
                    hidden(l, t1, 1)
                message(l, i, 6)
                message(l, i, 7)
                if nodes:
                    deviation(l, t1, 1)
                    features(l, t1, 1)

            with act.If(general == 0):
                with act.Fori(0, LAYERS) as l:
                    wait_alone(act, "act", x_ready, (l + 1) * NODE_TILES)
                    nc.scalar.activation(w1_cur[:, :], one(w1_all, l), ACT.Copy).then_inc(w1_ready, 1)
                    body(l, 0, False)
                    with act.Fori(1, BODIES) as i:
                        body(l, i, True)
                    last = ((NODE_TILES - 2, 0), (NODE_TILES - 1, 1))
                    for stage in (scaled, hidden, deviation, features):
                        for t, h in last:
                            stage(l, t, h, NODE_TILES - 1)
            with act.Else():
                with act.Fori(0, LAYERS) as l:
                    wait_alone(act, "act", x_ready, (l + 1) * NODE_TILES)
                    nc.scalar.activation(result, x_cur[:, :, :], ACT.Identity,
                                         scale=eps1[0:NT, bass.ds(l, 1)]).then_inc(x_eps_ready, 1)
                    with act.Fori(0, BODIES) as i:
                        for k in range(SLOTS):
                            act.wait_ge(g_taken, l * QUADS + i * SLOTS + (SLOTS + k + 1))
                            nc.scalar.activation(msg[:, k % 2, :], pre[:, k % 2, :], ACT.Relu).then_inc(g_msg, 1)
                            if k % BLOCK_QUADS == BLOCK_QUADS - 1:
                                load_attr(act, i + 1, k // BLOCK_QUADS)
                    step = l * 6
                    wait_alone(act, "act", g_layer, l + 1)
                    nc.scalar.activation(w1_cur[:, :], one(w1_all, l), ACT.Copy).then_inc(w1_ready, 1)
                    for g, ts in enumerate(groups()):
                        n = (ts.stop - ts.start) * NT
                        ins = nc.scalar.activation(zT_all[:, g * GROUP_COLS:g * GROUP_COLS + n], bank(g, n), ACT.Copy)
                    ins.then_inc(g_step, 1)
                    wait_alone(act, "act", g_step, step + 2)
                    for g, ts in enumerate(groups()):
                        n = (ts.stop - ts.start) * NT
                        ins = nc.scalar.activation(hT_all[:, g * GROUP_COLS:g * GROUP_COLS + n], bank(g, n), ACT.Relu,
                                                   scale=bn_scale[:, bass.ds(l, 1)], bias=bn_bias[:, bass.ds(l, 1)])
                    ins.then_inc(g_step, 1)
                    act.wait_ge(var_ready, l + 1)
                    nc.scalar.activation(std[:, :], mean_var[:, :, 1], ACT.Sqrt, bias=eps_col[0:NT, :]).then_inc(std_ready, 1)
                    act.wait_ge(g_step, step + 5)
                    nc.scalar.activation(x_cur[:, :, :], result, ACT.Relu).then_inc(x_ready, NODE_TILES)
                    wait_alone(act, "act", x_ready, (l + 2) * NODE_TILES)
                    for n, table in enumerate(tables):
                        with act.If(l == n):
                            act.dma_start(table.rearrange("(t p) d -> p t d", p=NT), x_cur[:, :, :]
                                          ).then_inc(table_ready, 16)
                    act.sem_inc(g_step, 1)

            for g, ts in enumerate(groups()):
                act.wait_ge(last_var, g + 1)
                nc.scalar.activation(std[:, ts], mean_var[:, ts, 1], ACT.Sqrt, bias=eps_col[0:NT, :]).then_inc(last_std, 1)

        @block.vector
        def _(dve):
            done = [0]

            def step(ins):
                done[0] += 1
                ins.then_inc(dve_step, 1)
                dve.wait_ge(dve_step, done[0])

            nc.vector.memset(eps_col[:, :], EPS).then_inc(eps_ready, 1)
            nc.vector.memset(attr_t[EDGE_FEAT:EDGE_FEAT + 1, :, :], 1.0)
            nc.vector.memset(ones[:, :], 1.0)
            nc.vector.memset(zeros_b[:, :], 0.0)
            nc.vector.memset(b2_split[:, :, :], 0.0)
            step(nc.vector.memset(ones_b[:, :], 1.0))
            for semaphore, value in ((bank_taken, SLOTS), (flushed, 2),
                                     (g_filled, SLOTS), (g_taken, SLOTS), (g_used, 1)):
                dve.sem_inc(semaphore, value)

            dve.wait_ge(edges_loaded, 32)
            dve.wait_ge(iota_made, 3)
            nc.vector.tensor_copy(dst_f[:, :], dst_i[:, :])
            step(nc.vector.tensor_copy(first_f[:, :], first_i[:, :]))
            nc.vector.tensor_tensor(dst_rel[:, :], dst_f[:, :], first_f[:, :], ALU.subtract)
            step(nc.vector.tensor_tensor(col_f[:, :], first_f[:, 0:EDGE_TILES:QUAD], base_i[:, :], ALU.add))
            nc.vector.tensor_reduce(ends[:, 0:1], dst_rel[:, :], AX.X, ALU.max)
            nc.vector.tensor_reduce(ends[:, 1:2], dst_rel[:, :], AX.X, ALU.min)
            nc.vector.tensor_reduce(ends[:, 2:3], col_f[:, :], AX.X, ALU.max)
            step(nc.vector.tensor_reduce(ends[:, 3:4], col_f[:, :], AX.X, ALU.min))
            nc.vector.tensor_scalar(misfits[:, 0:1], ends[:, 0:1], float(WINDOW), None, ALU.is_ge)
            nc.vector.tensor_scalar(misfits[:, 1:2], ends[:, 1:2], 0.0, None, ALU.is_lt)
            nc.vector.tensor_scalar(misfits[:, 2:3], ends[:, 2:3], float(BANK_COLS - WINDOW), None, ALU.is_gt)
            step(nc.vector.tensor_scalar(misfits[:, 3:4], ends[:, 3:4], 0.0, None, ALU.is_lt))
            nc.vector.tensor_reduce(misfit[:, :], misfits[:, :], AX.X, ALU.add).then_inc(misfit_ready, 1)
            step(nc.vector.tensor_copy(col_i[:, :], col_f[:, :]))
            dve.wait_ge(misfit_sum, 1)
            nc.vector.tensor_copy(flag[:, :], ps[0:1, 0:1]).then_inc(flag_ready, 1)

            step(nc.vector.tensor_copy(iota_f[:, :], iota_i[:, :]))

            dve.wait_ge(weights_loaded, 16 * 7)
            dve.wait_ge(bn_std_ready, 1)
            step(nc.vector.reciprocal(bn_tmp[:, :], bn_std[:, :]))
            step(nc.vector.tensor_tensor(bn_scale[:, :], bn_tmp[:, :], vec[:, :, 1], ALU.mult))
            step(nc.vector.tensor_tensor(bn_tmp[:, :], vec[:, :, 0], vec[:, :, 3], ALU.subtract))
            step(nc.vector.tensor_tensor(bn_bias[:, :], bn_tmp[:, :], bn_scale[:, :], ALU.mult))
            step(nc.vector.tensor_tensor(bn_bias[:, :], bn_bias[:, :], vec[:, :, 2], ALU.add))
            step(nc.vector.tensor_scalar(eps1[:, :], vec[:, :, 5], 1.0, None, ALU.add))
            for n in range(B2_PARTS):
                left = b2_rows if n == 0 else b2_rest
                step(nc.vector.tensor_copy(b2_part[:, :, :], left[:, :, :]))
                step(nc.vector.scalar_tensor_tensor(b2_split[:, :, :], b2_part[:, :, :], ident[0:B2_PARTS, n:n + 1],
                                                    b2_split[:, :, :], ALU.mult, ALU.add))
                step(nc.vector.tensor_tensor(b2_rest[:, :, :], left[:, :, :], b2_part[:, :, :], ALU.subtract))
            dve.sem_inc(tables_ready, 1)
            general = dve.value_load(flag[0:1, 0:1])

            def add_rows(l, i, k):
                dve.wait_ge(bank_filled, turn(l, i, k))
                dve.wait_ge(gathered[k], (i + 1 + l * BODIES) * (16 * QUAD))
                nc.vector.tensor_tensor(pre[:, k % BUFFERS, :], bank(k % BUFFERS),
                                        rows[:, k, :, :].rearrange("p j d -> p (j d)"), ALU.add).then_inc(bank_taken, 1)

            def windows(l, i, k):
                nc.vector.tensor_tensor(
                    onehot[:, k % BUFFERS, :, :],
                    iota_f[:, 0:WINDOW].unsqueeze(1).to_broadcast([P, QUAD, WINDOW]),
                    dst_rel[:, bass.ds(i * BODY_TILES + k * QUAD, QUAD)].unsqueeze(2).to_broadcast([P, QUAD, WINDOW]),
                    ALU.is_equal).then_inc(onehot_ready, 1)

            def flush(l, s, h, first=False):
                dve.wait_ge(flushed, l * BLOCKS + (s + 2))
                dve.wait_ge(segment_done, l * BLOCKS + (s + 1))
                if first:
                    nc.vector.tensor_copy(z_sum[:, 0:BANK_COLS], z_bank(h)).then_inc(flushed, 1)
                    return
                nc.vector.tensor_tensor(z_sum[:, bass.ds(s * NT, OVERLAP)], z_sum[:, bass.ds(s * NT, OVERLAP)],
                                        z_bank(h)[:, 0:OVERLAP], ALU.add)
                nc.vector.tensor_copy(z_sum[:, bass.ds(s * NT + OVERLAP, NT)], z_bank(h)[:, OVERLAP:]).then_inc(flushed, 1)

            def node_sum(l, t, h, upto=None):
                dve.wait_ge(flushed, l * BLOCKS + ((BLOCKS if upto else t + 2) + 2))
                dve.wait_ge(xT_ready, node(l, upto or t))
                nc.vector.tensor_tensor(zT[:, h, :], zh_cols(h, 0), z_sum[:, bass.ds((t + 1) * NT, NT)],
                                        ALU.add).then_inc(z_ready, 1)

            def node_stats(l, t, h, upto=None):
                dve.wait_ge(y_ready, node(l, upto or t))
                nc.vector.bn_stats(stats[:, h, :], y_cols(h)).then_inc(stats_ready, 1)
                wait_alone(dve, "dve", stats_ready, node(l, t))
                nc.vector.bn_aggr(mean_var[:, h, :], stats[:, h, :]).then_inc(var_ready, 1)

            def node_norm(l, t, h, upto=None):
                dve.wait_ge(std_ready, node(l, t))
                nc.vector.reciprocal(rstd[:, h:h + 1], std[:, h:h + 1]).then_inc(rstd_ready, 1)
                dve.wait_ge(var_ready, node(l, t))
                nc.vector.scalar_tensor_tensor(norm[:, h, :], y_cols(h), mean_var[:, h, 0:1], g_rows[0:NT, :],
                                               ALU.subtract, ALU.mult).then_inc(rstd_ready, 1)
                dve.wait_ge(rstd_ready, node(l, t) * 2)
                nc.vector.scalar_tensor_tensor(norm[:, h, :], norm[:, h, :], rstd[:, h:h + 1], b_rows[0:NT, :],
                                               ALU.mult, ALU.add).then_inc(norm_ready, 1)

            def body(l, i, nodes):
                t0, t1 = i * 2 - 2, i * 2 - 1

                def quad(k):
                    add_rows(l, i, k)
                    windows(l, i, k)

                quad(0)
                quad(1)
                if nodes:
                    flush(l, i * 2 - 1, 1)
                    node_sum(l, t0, 0)
                quad(2)
                quad(3)
                if nodes:
                    node_stats(l, t0, 0)
                quad(4)
                if nodes:
                    node_norm(l, t0, 0)
                quad(5)
                flush(l, i * 2, 0, first=not nodes)
                if nodes:
                    node_sum(l, t1, 1)
                quad(6)
                quad(7)
                if nodes:
                    node_stats(l, t1, 1)
                    node_norm(l, t1, 1)

            with dve.If(general == 0):
                with dve.Fori(0, LAYERS) as l:
                    body(l, 0, False)
                    with dve.Fori(1, BODIES) as i:
                        body(l, i, True)
                    flush(l, BLOCKS - 1, 1)
                    last = ((NODE_TILES - 2, 0), (NODE_TILES - 1, 1))
                    for stage in (node_sum, node_stats, node_norm):
                        for t, h in last:
                            stage(l, t, h, NODE_TILES - 1)
            with dve.Else():
                with dve.Fori(0, LAYERS) as l:
                    with dve.Fori(0, BODIES) as i:
                        for k in range(SLOTS):
                            q = l * QUADS + i * SLOTS + k
                            dve.wait_ge(g_filled, q + (SLOTS + 1))
                            dve.wait_ge(gathered[k], (i + 1 + l * BODIES) * (16 * QUAD))
                            nc.vector.tensor_tensor(pre[:, k % 2, :], bank(7), rows[:, k, :, :].rearrange("p j d -> p (j d)"),
                                                    ALU.add).then_inc(g_taken, 1)
                            for j in range(QUAD):
                                for g in range(GROUPS):
                                    dve.wait_ge(g_used, (q * QUAD + j) * GROUPS + (g + 1))
                                    nc.vector.tensor_scalar(
                                        onehot_all[:, :], iota_f[:, 0:GROUP_COLS], float(g * GROUP_COLS),
                                        dst_f[:, bass.ds(i * BODY_TILES + (k * QUAD + j), 1)],
                                        ALU.add, ALU.is_equal).then_inc(g_hot, 1)
                    at = l * 6
                    dve.wait_ge(g_step, at + 4)
                    for g, ts in enumerate(groups()):
                        for t in range(ts.start, ts.stop):
                            c = g * BANK_COLS + (t - ts.start) * FEAT
                            ins = nc.vector.bn_stats(stats[:, t, :], ps[0:NT, c:c + FEAT])
                    ins.then_inc(stats_ready, 1)
                    wait_alone(dve, "dve", stats_ready, l + 1)
                    for t in range(NODE_TILES):
                        ins = nc.vector.bn_aggr(mean_var[:, t, :], stats[:, t, :])
                    ins.then_inc(var_ready, 1)
                    dve.wait_ge(std_ready, l + 1)
                    nc.vector.reciprocal(rstd[:, :], std[:, :]).then_inc(rstd_ready, 1)
                    for g, ts in enumerate(groups()):
                        for t in range(ts.start, ts.stop):
                            c = g * BANK_COLS + (t - ts.start) * FEAT
                            ins = nc.vector.scalar_tensor_tensor(
                                result[:, t, :], ps[0:NT, c:c + FEAT], mean_var[:, t, 0:1], g_rows[0:NT, :],
                                ALU.subtract, ALU.mult)
                    ins.then_inc(norm_ready, 1)
                    dve.wait_ge(rstd_ready, l + 1)
                    dve.wait_ge(norm_ready, l + 1)
                    for t in range(NODE_TILES):
                        ins = nc.vector.scalar_tensor_tensor(
                            result[:, t, :], result[:, t, :], rstd[:, t:t + 1], b_rows[0:NT, :], ALU.mult, ALU.add)
                    ins.then_inc(g_step, 1)

            dve.wait_ge(x_ready, (LAYERS + 1) * NODE_TILES)

            def last_stats(ts):
                step(nc.vector.tensor_tensor(x_in[:, ts, :], x_in[:, ts, :], x_cur[:, ts, :], ALU.add))
                for t in range(ts.start, ts.stop):
                    ins = nc.vector.bn_stats(stats[:, t, :], x_in[:, t, :])
                step(ins)
                for t in range(ts.start, ts.stop):
                    ins = nc.vector.bn_aggr(mean_var[:, t, :], stats[:, t, :])
                ins.then_inc(last_var, 1)

            def last_norm(g, ts):
                dve.wait_ge(last_std, g + 1)
                step(nc.vector.reciprocal(rstd[:, ts], std[:, ts]))
                for t in range(ts.start, ts.stop):
                    ins = nc.vector.tensor_scalar(result[:, t, :], x_in[:, t, :], mean_var[:, t, 0:1], rstd[:, t:t + 1],
                                                  ALU.subtract, ALU.mult)
                ins.then_inc(out_ready, 1)

            for g, ts in enumerate(groups()):
                last_stats(ts)
                if g >= 1:
                    last_norm(g - 1, groups()[g - 1])
            last_norm(GROUPS - 1, groups()[-1])

        @block.tensor
        def _(pe):
            pe.wait_ge(misfit_ready, 1)
            nc.tensor.matmul(ps[0:1, 0:1], misfit[:, :], ones[:, :], start=True, stop=True).then_inc(misfit_sum, 1)
            pe.wait_ge(tables_ready, 1)
            general = pe.value_load(flag[0:1, 0:1])

            def edge_term(l, k, j, cols):
                c = ((k % BLOCK_QUADS) * QUAD + j) * P
                return nc.tensor.matmul(cols, attr_t[:, k // BLOCK_QUADS, c:c + P], one(we, l),
                                        start=True, stop=True, skip_group_check=True)

            def edge_terms(l, i, k):
                i, k = i + k // SLOTS, k % SLOTS
                if k % BLOCK_QUADS == 0:
                    pe.wait_ge(attr_loaded[k // BLOCK_QUADS], (i + (1 + l * BODIES)) * 16)
                pe.wait_ge(bank_taken, turn(l, i, k) + (SLOTS - BUFFERS))
                for j in range(QUAD):
                    ins = edge_term(l, k, j, bank(k % BUFFERS)[:, j * FEAT:(j + 1) * FEAT])
                ins.then_inc(bank_filled, 1)

            def clear(l, i, h):
                pe.wait_ge(flushed, (l * BODIES + i) * 2 + (h + 1))
                nc.tensor.matmul(z_bank(h), ones_b[0:1, :], zeros_b[:, :], start=True, stop=False, skip_group_check=True)

            def scatter(l, i, k, cols):
                pe.wait_ge(onehot_ready, turn(l, i, k))
                pe.wait_ge(msg_ready, turn(l, i, k))
                h = k // BLOCK_QUADS
                for j in range(QUAD):
                    ins = nc.tensor.matmul(ps[:, bass.ds(cols[k] + (BUFFERS + h) * BANK_COLS, WINDOW)],
                                           msg[:, k % BUFFERS, j * FEAT:(j + 1) * FEAT], onehot[:, k % BUFFERS, j, :],
                                           start=False, stop=False, skip_group_check=True)
                if k % BLOCK_QUADS == BLOCK_QUADS - 1:
                    ins.then_inc(segment_done, 1)

            def transposed(l, t, h, upto=None):
                pe.wait_ge(x_eps_ready, node(l, t))
                nc.tensor.matmul(zh_cols(h, 0), x_eps[:, h, :], ident[0:NT, 0:NT],
                                 start=True, stop=True, skip_group_check=True).then_inc(xT_ready, 1)

            def hidden(l, t, h, upto=None):
                pe.wait_ge(w1_ready, l + 1)
                pe.wait_ge(z_ready, node(l, upto or t))
                nc.tensor.matmul(zh_cols(h, 1), w1_cur[:, :], zT[:, h, :],
                                 start=True, stop=True, skip_group_check=True).then_inc(h_ready, 1)

            def output(l, t, h, upto=None):
                wait_alone(pe, "pe", hT_ready, node(l, upto or t))
                nc.tensor.matmul(y_cols(h), ones_b[:, 0:NT], one(b2_split, l), start=True, stop=False, skip_group_check=True)
                nc.tensor.matmul(y_cols(h), hT[:, h, :], one(w2_all, l),
                                 start=False, stop=True, skip_group_check=True).then_inc(y_ready, 1)

            def body(l, i, nodes, ahead=True):
                t0, t1 = i * 2 - 2, i * 2 - 1
                _, cols = nc.values_load_multi_w_load_instructions(
                    col_i[0:1, bass.ds(i * SLOTS, SLOTS)], engines=[mybir.EngineType.PE],
                    min_val=0, max_val=BANK_COLS - WINDOW)

                def quad(k):
                    if k + AHEAD < SLOTS or ahead:
                        edge_terms(l, i, k + AHEAD)
                    scatter(l, i, k, cols)

                clear(l, i, 0)
                quad(0)
                if nodes:
                    transposed(l, t0, 0)
                quad(1)
                if nodes:
                    hidden(l, t0, 0)
                quad(2)
                if nodes:
                    output(l, t0, 0)
                quad(3)
                clear(l, i, 1)
                quad(4)
                if nodes:
                    transposed(l, t1, 1)
                quad(5)
                if nodes:
                    hidden(l, t1, 1)
                quad(6)
                if nodes:
                    output(l, t1, 1)
                quad(7)

            with pe.If(general == 0):
                with pe.Fori(0, LAYERS) as l:
                    for k in range(AHEAD):
                        edge_terms(l, 0, k)
                    body(l, 0, False)
                    with pe.Fori(1, BODIES - 1) as i:
                        body(l, i, True)
                    body(l, BODIES - 1, True, ahead=False)
                    last = ((NODE_TILES - 2, 0), (NODE_TILES - 1, 1))
                    for stage in (transposed, hidden, output):
                        for t, h in last:
                            stage(l, t, h, NODE_TILES - 1)
            with pe.Else():
                with pe.Fori(0, LAYERS) as l:
                    pe.wait_ge(x_eps_ready, l + 1)
                    for g, ts in enumerate(groups()):
                        for t in range(ts.start, ts.stop):
                            c = g * BANK_COLS + (t - ts.start) * NT
                            nc.tensor.matmul(ps[:, c:c + NT], result[:, t, :], ident[0:NT, 0:NT],
                                             start=t == ts.start, stop=False, skip_group_check=True)
                    with pe.Fori(0, BODIES) as i:
                        for k in range(SLOTS):
                            q = l * QUADS + i * SLOTS + k
                            if k % BLOCK_QUADS == 0:
                                pe.wait_ge(attr_loaded[k // BLOCK_QUADS], (i + 1 + l * BODIES) * 16)
                            pe.wait_ge(g_taken, q + SLOTS)
                            for j in range(QUAD):
                                ins = edge_term(l, k, j, bank(7)[:, j * FEAT:(j + 1) * FEAT])
                            ins.then_inc(g_filled, 1)
                            pe.wait_ge(g_msg, q + 1)
                            for j in range(QUAD):
                                for g in range(GROUPS):
                                    pe.wait_ge(g_hot, (q * QUAD + j) * GROUPS + (g + 1))
                                    nc.tensor.matmul(bank(g, GROUP_COLS), msg[:, k % 2, j * FEAT:(j + 1) * FEAT],
                                                     onehot_all[:, :], start=False, stop=False,
                                                     skip_group_check=True).then_inc(g_used, 1)
                    pe.wait_ge(g_used, (l + 1) * (EDGE_TILES * GROUPS) + 1)
                    pe.sem_inc(g_layer, 1)
                    at = l * 6
                    pe.wait_ge(w1_ready, l + 1)
                    pe.wait_ge(g_step, at + 1)
                    for g, ts in enumerate(groups()):
                        n = (ts.stop - ts.start) * NT
                        ins = nc.tensor.matmul(bank(g, n), w1_cur[:, :], zT_all[:, g * GROUP_COLS:g * GROUP_COLS + n],
                                               start=True, stop=True, skip_group_check=True)
                    ins.then_inc(g_step, 1)
                    wait_alone(pe, "pe", g_step, at + 3)
                    for g, ts in enumerate(groups()):
                        n = ts.stop - ts.start
                        nc.tensor.matmul(ps[0:NT, g * BANK_COLS:g * BANK_COLS + n * FEAT], ones_b[:, 0:NT],
                                         b2_split[:, bass.ds(l, 1), :].to_broadcast([B2_PARTS, n, FEAT]),
                                         start=True, stop=False, skip_group_check=True)
                        for t in range(ts.start, ts.stop):
                            c = g * BANK_COLS + (t - ts.start) * FEAT
                            ins = nc.tensor.matmul(ps[0:NT, c:c + FEAT], hT_all[:, t * NT:(t + 1) * NT], one(w2_all, l),
                                                   start=False, stop=t == ts.stop - 1, skip_group_check=True)
                    ins.then_inc(g_step, 1)


def kernel(**inputs):
    import numpy as np
    import concourse.bacc as bacc
    from concourse.bass_utils import run_bass_kernel_spmd

    def pad(a, n, value=0):
        a = np.asarray(a)
        filled = np.full((n,) + a.shape[1:], value, a.dtype)
        filled[:a.shape[0]] = a
        return filled

    def rows(name, n):
        a = np.asarray(inputs[name])
        return np.ascontiguousarray(np.broadcast_to(a[None], (n,) + a.shape))

    def twice(blocks):
        return np.concatenate([blocks, blocks[:BLOCKS_IN_BODY]])

    dst = pad(inputs["dst"], EDGES_PAD, NODES).reshape(EDGE_TILES, P)
    src = pad(inputs["src"], EDGES_PAD)
    attr = pad(inputs["edge_attr_64"], EDGES_PAD)
    eps = np.broadcast_to(np.asarray(inputs["L0_gnn_eps"])[:, None], (LAYERS, FEAT))
    columns = [inputs["L0_gnn_" + k] for k in ("b1", "bn_g", "bn_b", "bn_mean", "bn_var")] + [eps]
    arrays = {
        "x": pad(inputs["x"], NODES_PAD),
        "attr": twice(attr.reshape(BLOCKS, BLOCK_TILES * P, EDGE_FEAT).transpose(0, 2, 1)).reshape(-1, BLOCK_TILES * P),
        "src": twice(src.reshape(BLOCKS, BLOCK_TILES, P).transpose(0, 2, 1)).reshape(-1, BLOCK_TILES),
        "dst": dst.T,
        "dst_first": np.broadcast_to(np.repeat(dst[::QUAD, 0], QUAD), (P, EDGE_TILES)),
        "edge_w": np.concatenate([np.asarray(inputs["L0_gnn_edge_W"]),
                                  np.asarray(inputs["L0_gnn_edge_b"])[:, None]], 1).transpose(1, 0, 2),
        "vecs": np.stack([np.asarray(c) for c in columns], -1).transpose(1, 0, 2),
        "w1": np.asarray(inputs["L0_gnn_W1"]).transpose(1, 0, 2),
        "w2": np.asarray(inputs["L0_gnn_W2"]).transpose(1, 0, 2),
        "b2": rows("L0_gnn_b2", B2_PARTS),
        "ln_g": rows("L0_gnn_ln_g", P),
        "ln_b": rows("L0_gnn_ln_b", P),
    }
    arrays = {k + "_dram": np.ascontiguousarray(v) for k, v in arrays.items()}
    nc = bacc.Bacc("TRN2", target_bir_lowering=False, num_devices=1)
    args = [nc.dram_tensor(k, v.shape, mybir.dt.from_np(v.dtype), kind="ExternalInput").ap() for k, v in arrays.items()]
    tables = [nc.dram_tensor(f"table{n}_dram", (NODES_PAD, FEAT), mybir.dt.float32, kind="Internal").ap()
              for n in range(LAYERS - 1)]
    out = nc.dram_tensor("out_dram", (NODES_PAD, FEAT), mybir.dt.float32, kind="ExternalOutput").ap()
    build(nc, *args, tables, out)
    result = run_bass_kernel_spmd(nc, [arrays], core_ids=[0])
    return result.results[0]["out_dram"][:NODES]
```
